# Optimizing a Trainium2 kernel written in Bass

```python
import numpy as np
import jax
import jax.numpy as jnp

def _softmax(x, axis=-1):
    return jax.nn.softmax(x, axis=axis)

def _gelu(x):
    return jax.nn.gelu(x, approximate=True)

def _silu(x):
    return jax.nn.silu(x)

def _sigmoid(x):
    return jax.nn.sigmoid(x)

def _layernorm(x, axis=-1, eps=1e-05):
    m = jnp.mean(x, axis=axis, keepdims=True)
    v = jnp.var(x, axis=axis, keepdims=True)
    return (x - m) / jnp.sqrt(v + eps)

def _scatter_add(tgt, idx, src, axis=0):
    return tgt.at[idx].add(src)

def _segment_sum(src, seg, n):
    return jax.ops.segment_sum(src, seg, n)
kernel_name = 'mk_adaln_ffn_d1_seqx_r8_f71a4a'

def setup_inputs(seed: int=0):
    np.random.seed(seed)
    _w = jnp.asarray

    def _rec_inputs():
        import jax
        import jax.numpy as jnp
        _rk = jax.random.key(seed)
        x = -8.015e-05 + 0.9999 * jax.random.normal(jax.random.fold_in(_rk, 1), (128, 32, 256), jnp.float32)
        _lenS = 32 - jax.random.randint(jax.random.fold_in(_rk, 7), (128,), 0, max(1, 32 // 4) + 1, jnp.int32)
        _lenS2 = 32 - jax.random.randint(jax.random.fold_in(_rk, 8), (128,), 0, max(1, 32 // 4) + 1, jnp.int32)
        cond_1024 = 0.00191187 + 0.999416 * jax.random.normal(jax.random.fold_in(_rk, 11), (128, 128), jnp.float32)
        return (x, cond_1024)
    x, cond_1024 = _rec_inputs()

    def _L0_cond_setup():
        import jax, jax.numpy as jnp
        import numpy as np
        B, N, V_DIM, Q_DIM = (32, 100, 256, 128)
        key = jax.random.key(seed)
        k1, k2, k3, k4 = jax.random.split(key, 4)
        v = jax.random.normal(k1, (B, N, V_DIM), dtype=jnp.float32)
        q = jax.random.normal(k2, (B, Q_DIM), dtype=jnp.float32)
        W3 = jax.random.normal(k3, (Q_DIM, V_DIM), dtype=jnp.float32) * (1.0 / np.sqrt(Q_DIM))
        b3 = jnp.zeros((V_DIM,), dtype=jnp.float32)
        W2 = jax.random.normal(k4, (V_DIM, V_DIM), dtype=jnp.float32) * (1.0 / np.sqrt(V_DIM))
        b2 = jnp.zeros((V_DIM,), dtype=jnp.float32)
        return {'v': v, 'q': q, 'W3': W3, 'b3': b3, 'W2': W2, 'b2': b2}
    _L0_cond_all = _L0_cond_setup()
    _L0_cond_in = {k: v for k, v in _L0_cond_all.items() if k in ('W3', 'b3', 'W2', 'b2')}
    del _L0_cond_all

    def _L0_ffn_setup():
        import jax, jax.numpy as jnp
        import numpy as np
        D_MODEL = 256
        HIDDEN = int(2 * D_MODEL * 4 / 3)

        def ternary_quant(w):
            s = jnp.mean(jnp.abs(w))
            q = jnp.clip(jnp.round(w / s), -1.0, 1.0) * s
            return w + jax.lax.stop_gradient(q - w)
        key = jax.random.key(seed)
        k0, k1, k2, k3 = jax.random.split(key, 4)
        x = jax.random.normal(k0, (4, 512, D_MODEL), dtype=jnp.float32)
        std_in = 1.0 / np.sqrt(D_MODEL)
        std_h = 1.0 / np.sqrt(HIDDEN)
        w1 = jax.random.uniform(k1, (HIDDEN, D_MODEL), jnp.float32, -std_in, std_in)
        w3 = jax.random.uniform(k2, (HIDDEN, D_MODEL), jnp.float32, -std_in, std_in)
        w2 = jax.random.uniform(k3, (D_MODEL, HIDDEN), jnp.float32, -std_h, std_h)
        return {'x': x, 'w1': w1, 'w3': w3, 'w2': w2}
    _L0_ffn_all = _L0_ffn_setup()
    _L0_ffn_in = {k: v for k, v in _L0_ffn_all.items() if k in ('w1', 'w3', 'w2')}
    del _L0_ffn_all
    return {'x': x, 'cond_1024': cond_1024, 'L0_cond_W3': _L0_cond_in['W3'], 'L0_cond_b3': _L0_cond_in['b3'], 'L0_cond_W2': _L0_cond_in['W2'], 'L0_cond_b2': _L0_cond_in['b2'], 'L0_ffn_w1': _L0_ffn_in['w1'], 'L0_ffn_w3': _L0_ffn_in['w3'], 'L0_ffn_w2': _L0_ffn_in['w2']}

def reference(x, cond_1024, L0_cond_W3, L0_cond_b3, L0_cond_W2, L0_cond_b2, L0_ffn_w1, L0_ffn_w3, L0_ffn_w2):
    import jax
    import jax.numpy as jnp

    def _L0_cond_ref(v, q, W3, b3, W2, b2):
        import jax, jax.numpy as jnp
        import numpy as np
        B, N, V_DIM, Q_DIM = (32, 100, 256, 128)
        q_emb = jax.nn.relu(q @ W3 + b3)
        n = v.shape[1]
        v_sum = jnp.sum(v, axis=1, keepdims=True)
        x = (n * v + v_sum) * q_emb[:, None, :]
        return jax.nn.relu(x @ W2 + b2)

    def _L0_ffn_ref(x, w1, w3, w2):
        import jax, jax.numpy as jnp
        import numpy as np
        D_MODEL = 256
        HIDDEN = int(2 * D_MODEL * 4 / 3)

        def ternary_quant(w):
            s = jnp.mean(jnp.abs(w))
            q = jnp.clip(jnp.round(w / s), -1.0, 1.0) * s
            return w + jax.lax.stop_gradient(q - w)
        w1q = ternary_quant(w1)
        w3q = ternary_quant(w3)
        w2q = ternary_quant(w2)
        h1 = jnp.einsum('bsd,hd->bsh', x, w1q)
        h3 = jnp.einsum('bsd,hd->bsh', x, w3q)
        g = jax.nn.silu(h1) * h3
        return jnp.einsum('bsh,dh->bsd', g, w2q)
    x = x + _L0_ffn_ref(_L0_cond_ref(x, cond_1024, L0_cond_W3, L0_cond_b3, L0_cond_W2, L0_cond_b2), L0_ffn_w1, L0_ffn_w3, L0_ffn_w2)
    return x

_drawn_inputs = setup_inputs


def setup_inputs(seed=0):
    import zlib

    import numpy as np

    out = dict(_drawn_inputs(seed))
    spreads = {'L0_cond_b3': (0.0, 0.1), 'L0_cond_b2': (0.0, 0.8)}
    factors = {}
    for name, (base, spread) in spreads.items():
        noise = np.random.default_rng([zlib.crc32(name.encode()), seed]).standard_normal(out[name].shape)
        drawn = base * np.exp(spread * noise) if base else spread * noise
        out[name] = jnp.asarray(drawn.astype(out[name].dtype))
    for name, factor in factors.items():
        out[name] = (out[name] * factor).astype(out[name].dtype)
    return out
```

```python
from contextlib import ExitStack

import concourse.bass as bass
from concourse import mybir

F32 = mybir.dt.float32
F32R = mybir.dt.float32r
BF16 = mybir.dt.bfloat16
ALU = mybir.AluOpType
ACT = mybir.ActivationFunctionType
AX = mybir.AxisListType

P = 128
BANK = 512


def adaln_ternary_ffn_kernel(nc, x, cond, W3, b3, W2, b2, w1, w3, w2, out):
    B, S, D = x.shape
    Q = cond.shape[1]
    H = w1.shape[0]
    DC = D // P
    HC = H // P
    HR = H - HC * P
    HR2 = 64
    RM = HR2 + HR
    STEPS = HC + 1
    GT = BANK
    NG = B * S // GT
    GB = GT // S
    TT = GT // P
    W_COUNT = float(H * D)
    assert B == P and Q == P and HR <= 32 + 10 and 2 * HR <= P and NG == 8 and GT % S == 0

    x_v = x.rearrange("b s d -> (b s) d").rearrange("(g t p) d -> g p t d", t=TT, p=P)
    out_v = out.rearrange("b s d -> (b s) d").rearrange("(g t p) d -> g p t d", t=TT, p=P)

    with ExitStack() as ctx:
        def sb(name, shape, dt):
            return ctx.enter_context(nc.sbuf_tensor(name, shape, dt))

        def sem(name):
            return ctx.enter_context(nc.semaphore(name))

        cond_sb = sb("cond_sb", [P, Q], F32)
        condT = sb("condT", [P, B], F32)
        W3_sb = sb("W3_sb", [P, D], F32)
        W2_sb = sb("W2_sb", [P, DC, D], F32)
        b3_sb = sb("b3_sb", [P, DC], F32)
        b2_sb = sb("b2_sb", [P, DC], F32)
        qT = sb("qT", [P, NG, DC, GB], F32)
        w1_sb = sb("w1_sb", [P, STEPS, D], F32)
        w3_sb = sb("w3_sb", [P, STEPS, D], F32)
        w2_sb = sb("w2_sb", [P, DC, H], F32)
        w1_t = sb("w1_t", [P, STEPS, D], BF16)
        w3_t = sb("w3_t", [P, STEPS, D], BF16)
        w2_t = sb("w2_t", [P, DC, H], BF16)
        below = sb("below", [P, STEPS * D], BF16)
        abs_sums = sb("abs_sums", [P, 6], F32)
        scales = sb("scales", [P, 3], F32)
        limits = sb("limits", [P, 3], F32)
        neg_limits = sb("neg_limits", [P, 3], F32)
        inverse = sb("inverse", [P, 3], F32)
        checked = sb("checked", [P, 3], F32)
        out_scale = sb("out_scale", [P, 1], F32)
        T13 = sb("T13", [P, DC, 2 * HC * P + P], F32R)
        T2 = sb("T2", [P, STEPS, D], F32R)
        ident = sb("ident", [P, P], F32)
        ident16 = sb("ident16", [P, P], BF16)
        ones = sb("ones", [P, P], F32)
        xs = [sb(f"xs{u}", [P, TT, D], F32) for u in range(2)]
        vsum = [sb(f"vsum{u}", [P, DC, GB], F32) for u in range(2)]
        y = [sb(f"y{u}", [P, DC, GT], F32) for u in range(2)]
        x1 = [sb(f"x1{u}", [P, DC, GT], F32) for u in range(2)]
        ct = [sb(f"ct{u}", [P, DC, GT], F32) for u in range(2)]
        c_hi = sb("c_hi", [P, NG, DC, GT], F32R)
        c_lo = sb("c_lo", [P, NG, DC, GT], F32R)
        silu = [y[u][:, 0, :] for u in range(2)]
        gf = [y[0][:, 1, :], y[1][:, 1, :], x1[0][:, 0, :]]
        g_hi = [sb(f"g_hi{j}", [P, GT], F32R) for j in range(HC)]
        g_lo = [sb(f"g_lo{j}", [P, GT], F32R) for j in range(HC)]
        g_rest = sb("g_rest", [P, GT], F32R)
        xo = sb("xo", [P, NG, TT, D], F32)

        bank = ctx.enter_context(nc.psum_tensor("bank", [P, 8, BANK], F32))
        xT = [bank[:, 2 * u:2 * u + DC, :] for u in range(2)]
        z = [bank[:, 4 + c, :] for c in range(DC)]
        h1 = [bank[:, 2 * s, :] for s in range(3)]
        h3 = [bank[:, 2 * s + 1, :] for s in range(3)]
        o = [bank[:, 6 + b, :].rearrange("p (t d) -> p t d", t=2) for b in range(TT // 2)]
        condT_ps = bank[:, 4, 0:B]
        qT_ps = bank[:, 5, 0:DC * B].rearrange("p (c b) -> p c b", c=DC)
        sums_ps = bank[:, 6, 0:6]
        w_ps = [bank[:, 6 + b, :].bitcast(BF16) for b in range(2)]

        got_cond, got_W3, got_W2, got_b = sem("got_cond"), sem("got_W3"), sem("got_W2"), sem("got_b")
        got_w1, got_w3, got_w2 = sem("got_w1"), sem("got_w3"), sem("got_w2")
        got_xs = [sem(f"got_xs{u}") for u in range(2)]
        got_xo = sem("got_xo")
        stored = sem("stored")
        const_ready = sem("const_ready")
        zero_ready = sem("zero_ready")
        condT_done, condT_copied, q_done, q_ready = (sem("condT_done"), sem("condT_copied"), sem("q_done"),
                                                     sem("q_ready"))
        abs_done, sums_done, scale_step = sem("abs_done"), sem("sums_done"), sem("scale_step")
        below_done, ternary_done = sem("below_done"), sem("ternary_done")
        wT_done, wT_copied = sem("wT_done"), sem("wT_copied")
        xT_done = sem("xT_done")
        vsum_done = sem("vsum_done")
        y_done = sem("y_done")
        x1_done = sem("x1_done")
        z_done = sem("z_done")
        ct_done = sem("ct_done")
        c_hi_done = sem("c_hi_done")
        ct_free = sem("ct_free")
        h1_done, h3_done = sem("h1_done"), sem("h3_done")
        silu_done, g_done, g_hi_done, g_lo_done = sem("silu_done"), sem("g_done"), sem("g_hi_done"), sem("g_lo_done")
        o_done = [sem(f"o_done{b}") for b in range(2)]
        o_read = [sem(f"o_read{b}") for b in range(2)]

        block = ctx.enter_context(nc.Block())

        def group_batches(ap):
            return ap.rearrange("p c (b s) -> p (c b) s", s=S)

        def over_sequence(ap):
            return ap.unsqueeze(2).broadcast_to([P, DC * GB, S])

        def at(g):
            return g if isinstance(g, int) else bass.ds(g, 1)

        def group_of(tensor, g):
            return tensor[:, g] if isinstance(g, int) else \
                tensor[:, bass.ds(g, 1)].rearrange("p a c n -> p (a c) n")

        def rows_of(j):
            return slice(0, P) if j < HC else slice(0, HR)

        def later(g, j, by):
            return (g, j + by) if j + by < STEPS else (g + 1, j + by - STEPS)

        def h3_of(j):
            return h3[j % 3]

        @block.sync
        def _(sp):
            sp.sem_inc(ct_free, 2)
            sp.dma_start(cond_sb[:], cond).then_inc(got_cond, 16)
            sp.dma_start(W3_sb[:], W3).then_inc(got_W3, 16)
            sp.dma_start(xs[0][:], x_v[0]).then_inc(got_xs[0], 16)
            sp.dma_start(W2_sb[:], W2.rearrange("(c p) n -> p c n", p=P)).then_inc(got_W2, 16)
            sp.dma_start(xs[1][:], x_v[1]).then_inc(got_xs[1], 16)
            for w_sb, w, got in ((w1_sb, w1, got_w1), (w3_sb, w3, got_w3)):
                sp.dma_start(w_sb[:, 0:HC, :], w[0:HC * P, :].rearrange("(j p) d -> p j d", p=P)).then_inc(got, 16)
                sp.dma_start(w_sb[0:HR, HC, :], w[HC * P:H, :]).then_inc(got, 16)
            sp.dma_start(w2_sb[:], w2.rearrange("(c p) h -> p c h", p=P)).then_inc(got_w2, 16)
            with sp.Fori(0, NG // 2 - 1) as i:
                for u in range(2):
                    sp.wait_ge(xT_done, i * 2 + u + 1)
                    sp.dma_start(xs[u][:], x_v[bass.ds(i * 2 + u + 2, 1)].rearrange("a p t d -> p (a t) d")
                                 ).then_inc(got_xs[u], 16)
            for g in range(NG):
                sp.dma_start(xo[:, g], x_v[g]).then_inc(got_xo, 16)
            with sp.Fori(0, NG) as g:
                sp.wait_ge(o_read[0], g + 1)
                sp.wait_ge(o_read[1], g + 1)
                sp.dma_start(out_v[bass.ds(g, 1)].rearrange("a p t d -> p (a t) d"),
                             xo[:, bass.ds(g, 1)].rearrange("p a t d -> p (a t) d")).then_inc(stored, 16)
            sp.wait_ge(stored, 16 * NG)

        @block.gpsimd
        def _(pool):
            for c in range(DC):
                pool.dma_start(b3_sb[:, c:c + 1], b3[c * P:(c + 1) * P].rearrange("(p a) -> p a", a=1)).then_inc(got_b, 16)
                pool.dma_start(b2_sb[:, c:c + 1], b2[c * P:(c + 1) * P].rearrange("(p a) -> p a", a=1)).then_inc(got_b, 16)
            nc.gpsimd.memset(ident[:], 0.0).then_inc(const_ready, 1)
            pool.wait_ge(const_ready, 1)
            nc.gpsimd.affine_select(out=ident[:], in_=ident[:], compare_op=ALU.not_equal, fill=1.0, base=0,
                                    pattern=[[-1, P]], channel_multiplier=1).then_inc(const_ready, 1)
            pool.wait_ge(const_ready, 2)
            nc.gpsimd.tensor_copy(ident16[:], ident[:]).then_inc(const_ready, 1)
            nc.gpsimd.memset(ones[:], 1.0).then_inc(const_ready, 1)
            nc.gpsimd.memset(abs_sums[:], 0.0).then_inc(zero_ready, 1)
            nc.gpsimd.memset(T13[:, :, 2 * HC * P:].bitcast(F32), 0.0).then_inc(zero_ready, 1)
            nc.gpsimd.memset(T2[:, HC, :].bitcast(F32), 0.0).then_inc(zero_ready, 1)
            nc.gpsimd.memset(g_rest[:].bitcast(F32), 0.0).then_inc(zero_ready, 1)

            def scale_by_q(g, u):
                pool.wait_ge(y_done, g + 1)
                qg = group_of(qT, g)
                nc.gpsimd.tensor_tensor(group_batches(x1[u][:]), group_batches(y[u][:]),
                                        over_sequence(qg.rearrange("p c b -> p (c b)")), ALU.mult).then_inc(x1_done, 1)

            pool.wait_ge(q_ready, DC)
            with pool.Fori(0, NG // 2) as i:
                for u in range(2):
                    scale_by_q(i * 2 + u, u)

        @block.scalar
        def _(act):
            act.wait_ge(condT_done, 1)
            nc.scalar.copy(condT[:], condT_ps).then_inc(condT_copied, 1)
            act.wait_ge(got_b, 16 * 4)
            act.wait_ge(q_done, DC)
            for c in range(DC):
                nc.scalar.activation(qT[:, :, c, :], qT_ps[:, c, :].rearrange("p (g b) -> p g b", b=GB), ACT.Relu,
                                     bias=b3_sb[:, c:c + 1]).then_inc(q_ready, 1)
            act.wait_ge(zero_ready, 1)
            n = 0
            for k, (w_sb, got) in enumerate(((w1_sb, got_w1), (w3_sb, got_w3))):
                act.wait_ge(got, 32)
                for part, col in ((w_sb[:, 0:HC, :], 2 * k), (w_sb[0:HR, HC:STEPS, :], 2 * k + 1)):
                    rows = part.shape[0]
                    if n:
                        act.wait_ge(abs_done, n)
                    nc.scalar.activation(below[0:rows, 0:part.shape[1] * D].rearrange("p (j d) -> p j d", d=D), part,
                                         ACT.Abs, accum_out=abs_sums[0:rows, col:col + 1]).then_inc(abs_done, 1)
                    n += 1
            act.wait_ge(got_w2, 16)
            act.wait_ge(abs_done, n)
            nc.scalar.activation(below[:, 0:DC * H], w2_sb[:].rearrange("p c h -> p (c h)"), ACT.Abs,
                                 accum_out=abs_sums[:, 4:5]).then_inc(abs_done, 1)

            def relu_and_hi(g, u):
                act.wait_ge(ct_free, g + 1)
                for c in range(DC):
                    act.wait_ge(z_done, g * DC + c + 1)
                    nc.scalar.activation(ct[u][:, c, :], z[c], ACT.Relu, bias=b2_sb[:, c:c + 1]).then_inc(ct_done, 1)
                act.wait_ge(ct_done, g * DC + DC)
                nc.scalar.copy(group_of(c_hi, g), ct[u][:]).then_inc(c_hi_done, 1)

            with act.Fori(0, NG // 4) as i:
                for u in range(2):
                    relu_and_hi(i * 2 + u, u)
            for g in range(NG // 2, NG - 2):
                relu_and_hi(g, g % 2)
            act.wait_ge(zero_ready, 4)
            for k in range(2):
                act.wait_ge(wT_done, k + 1)
                for c in range(DC):
                    nc.scalar.copy(T13[:, c, k * HC * P:(k + 1) * HC * P], w_ps[c][:, 0:HC * P])
                    nc.scalar.copy(T13[:, c, 2 * HC * P + k * HR2:2 * HC * P + k * HR2 + HR],
                                   w_ps[c][:, HC * P:H]).then_inc(wT_copied, 1)
            for g in range(NG - 2, NG):
                relu_and_hi(g, g % 2)
            act.wait_ge(wT_done, 3)
            half = STEPS // 2
            nc.scalar.copy(T2[:, 0:half, :], w_ps[0][:, 0:half * D].rearrange("p (j d) -> p j d", d=D)
                           ).then_inc(wT_copied, 1)
            nc.scalar.copy(T2[:, half:HC, :], w_ps[1][:, 0:(HC - half) * D].rearrange("p (j d) -> p j d", d=D)
                           ).then_inc(wT_copied, 1)
            for row in (0, HR2):
                nc.scalar.copy(T2[row:row + HR, HC, :], w_ps[1][0:HR, (HC - half) * D:STEPS * D - half * D]
                               ).then_inc(wT_copied, 1)

            def silu_step(g, j):
                r = rows_of(j)
                act.wait_ge(h1_done, g * STEPS + j + 1)
                nc.scalar.activation(silu[j % 2][r], h1[j % 3][r], ACT.Silu, scale=checked[r, 0:1]
                                     ).then_inc(silu_done, 1)

            def hi_step(g, j):
                act.wait_ge(g_done, g * STEPS + j + 1)
                nc.scalar.copy(g_hi[j][:] if j < HC else g_rest[0:HR, :], gf[j % 3][rows_of(j)]).then_inc(g_hi_done, 1)

            act.wait_ge(scale_step, 5)
            silu_step(0, 0)
            with act.Fori(0, NG - 1) as g:
                for j in range(STEPS):
                    silu_step(*later(g, j, 1))
                    hi_step(g, j)
            for j in range(STEPS):
                if j + 1 < STEPS:
                    silu_step(NG - 1, j + 1)
                hi_step(NG - 1, j)

        @block.tensor
        def _(pe):
            pe.wait_ge(got_cond, 16)
            pe.wait_ge(const_ready, 4)
            pe.transpose(condT_ps, cond_sb[:], ident[:]).then_inc(condT_done, 1)
            pe.wait_ge(got_W3, 16)
            pe.wait_ge(condT_copied, 1)
            for c in range(DC):
                pe.matmul(qT_ps[:, c, :], W3_sb[:, c * P:(c + 1) * P], condT[:], start=True, stop=True
                          ).then_inc(q_done, 1)

            def transpose_x(u, load):
                pe.wait_ge(got_xs[u], load * 16 + 16)
                for c in range(DC):
                    for t in range(TT):
                        last = pe.transpose(xT[u][:, c, t * P:(t + 1) * P], xs[u][:, t, c * P:(c + 1) * P], ident[:])
                last.then_inc(xT_done, 1)

            def project_c(g, u):
                pe.wait_ge(x1_done, g + 1)
                pe.wait_ge(ct_done, g * DC)
                for c in range(DC):
                    for k in range(DC):
                        last = pe.matmul(z[c], W2_sb[:, k, c * P:(c + 1) * P], x1[u][:, k, :],
                                         start=(k == 0), stop=(k == DC - 1))
                    last.then_inc(z_done, 1)

            transpose_x(0, 0)
            transpose_x(1, 0)
            pe.wait_ge(abs_done, 5)
            pe.matmul(sums_ps[:, 0:5], ones[:], abs_sums[:, 0:5], start=True, stop=True).then_inc(sums_done, 1)
            pe.wait_ge(got_W2, 16)
            pe.wait_ge(q_ready, DC)
            with pe.Fori(0, NG // 4) as i:
                for u in range(2):
                    project_c(i * 2 + u, u)
                    pe.wait_ge(y_done, i * 2 + u + 1)
                    transpose_x(u, i + 1)
            for g in range(NG // 2, NG - 2):
                project_c(g, g % 2)
                pe.wait_ge(y_done, g + 1)
                transpose_x(g % 2, g // 2 + 1)

            def transpose_w(k, w_t):
                pe.wait_ge(ternary_done, k + 1)
                for c in range(DC):
                    pe.wait_ge(scale_step, 1) if k == 0 else pe.wait_ge(wT_copied, c + 1)
                    for j in range(STEPS):
                        rows = P if j < HC else HR
                        last = pe.transpose(w_ps[c][:, j * P:j * P + rows], w_t[0:rows, j, c * P:(c + 1) * P],
                                            ident16[0:rows, 0:rows])
                last.then_inc(wT_done, 1)

            transpose_w(0, w1_t)
            transpose_w(1, w3_t)
            project_c(NG - 2, 0)
            project_c(NG - 1, 1)
            pe.wait_ge(ternary_done, 3)
            pe.wait_ge(wT_copied, 2 * DC)
            half = STEPS // 2
            for j in range(STEPS):
                rows = P if j < HC else HR
                for c in range(DC):
                    last = pe.transpose(w_ps[j // half][0:rows, (j % half) * D + c * P:(j % half) * D + (c + 1) * P],
                                        w2_t[:, c, j * P:j * P + rows], ident16[:])
            last.then_inc(wT_done, 1)

            def hidden_step(g, j):
                w = P if j < HC else RM
                products = [(h1, j * P, h1_done), (h3, (HC + j) * P, h3_done)] if j < HC else \
                    [(h1, 2 * HC * P, h1_done)]
                passes = [(k, part) for k in range(DC) for part in (c_hi, c_lo)]
                for dst, col, done in products:
                    for i, (k, part) in enumerate(passes):
                        moving = part[:, at(g), k, :]
                        last = pe.matmul(dst[j % 3][0:w, :], T13[:, k, col:col + w], moving,
                                         start=(i == 0), stop=(i == len(passes) - 1))
                    last.then_inc(done, 1)

            def output_step(g, j):
                pe.wait_ge(g_lo_done, g * STEPS + j + 1)
                parts = [(g_hi[j], P), (g_lo[j], P)] if j < HC else [(g_rest, RM)]
                for b in range(TT // 2):
                    if j == 0:
                        pe.wait_ge(o_read[b], g)
                    for i, (part, rows) in enumerate(parts):
                        for t in range(2):
                            col = (2 * b + t) * P
                            last = pe.matmul(o[b][:, t, :], part[0:rows, col:col + P], T2[0:rows, j, :],
                                             start=(j == 0 and i == 0 and t == 0), stop=(j == HC),
                                             skip_group_check=True)
                    if j == HC:
                        last.then_inc(o_done[b], 1)

            pe.wait_ge(y_done, NG)
            pe.wait_ge(ct_done, NG * DC)
            pe.wait_ge(wT_copied, 2 * DC + 4)
            pe.wait_ge(ct_free, 2 + 1)
            hidden_step(0, 0)
            hidden_step(0, 1)
            with pe.Fori(0, NG - 1) as g:
                for j in range(STEPS):
                    if j == STEPS - 2:
                        pe.wait_ge(ct_free, g + 2 + 2)
                    pe.wait_ge(g_done, g * STEPS + j)
                    hidden_step(*later(g, j, 2))
                    output_step(g, j)
            for j in range(STEPS):
                if j + 2 < STEPS:
                    pe.wait_ge(g_done, (NG - 1) * STEPS + j)
                    hidden_step(NG - 1, j + 2)
                output_step(NG - 1, j)

        @block.vector
        def _(dve):
            def sum_and_add(g, u):
                dve.wait_ge(xT_done, g + 1)
                nc.vector.tensor_reduce(vsum[u][:].rearrange("p c b -> p (c b)"), group_batches(xT[u]), AX.X, ALU.add
                                        ).then_inc(vsum_done, 1)
                dve.wait_ge(vsum_done, g + 1)
                nc.vector.scalar_tensor_tensor(
                    out=group_batches(y[u][:]), in0=group_batches(xT[u]), scalar=float(S),
                    in1=over_sequence(vsum[u][:].rearrange("p c b -> p (c b)")), op0=ALU.mult, op1=ALU.add
                ).then_inc(y_done, 1)

            def lo_of_c(g, u):
                dve.wait_ge(c_hi_done, g + 1)
                nc.vector.tensor_tensor(group_of(c_lo, g), ct[u][:], group_of(c_hi, g).bitcast(F32), ALU.subtract
                                        ).then_inc(ct_free, 1)

            def ternary(k, w_sb, w_t, n, col):
                w, t = (a[:].rearrange("p a b -> p (a b)") for a in (w_sb, w_t))
                rows = [(0, P, 0, HC * D), (0, HR, HC * D, STEPS * D)] if k < 2 else [(0, P, 0, DC * H)]
                for r0, r1, a, b in rows:
                    nc.vector.tensor_scalar(below[r0:r1, a:b], w[r0:r1, a:b], neg_limits[r0:r1, col:col + 1], None,
                                            ALU.is_lt).then_inc(below_done, 1)
                dve.wait_ge(below_done, n)
                for i, (r0, r1, a, b) in enumerate(rows):
                    last = nc.vector.scalar_tensor_tensor(
                        out=t[r0:r1, a:b], in0=w[r0:r1, a:b], scalar=limits[r0:r1, col:col + 1],
                        in1=below[r0:r1, a:b], op0=ALU.is_gt, op1=ALU.subtract)
                last.then_inc(ternary_done, 1)

            sum_and_add(0, 0)
            sum_and_add(1, 1)
            dve.wait_ge(sums_done, 1)
            nc.vector.tensor_copy(abs_sums[:, 0:5], sums_ps[:, 0:5]).then_inc(scale_step, 1)
            dve.wait_ge(scale_step, 1)
            nc.vector.tensor_scalar(scales[:, 0:1], abs_sums[:, 0:1], abs_sums[:, 1:2], 1.0 / W_COUNT, ALU.add, ALU.mult)
            nc.vector.tensor_scalar(scales[:, 1:2], abs_sums[:, 2:3], abs_sums[:, 3:4], 1.0 / W_COUNT, ALU.add, ALU.mult)
            nc.vector.tensor_scalar(scales[:, 2:3], abs_sums[:, 4:5], 1.0 / W_COUNT, None, ALU.mult
                                    ).then_inc(scale_step, 1)
            dve.wait_ge(scale_step, 2)
            nc.vector.tensor_scalar(limits[:], scales[:], 0.5, None, ALU.mult)
            nc.vector.tensor_scalar(neg_limits[:], scales[:], -0.5, None, ALU.mult).then_inc(scale_step, 1)
            dve.wait_ge(scale_step, 3)
            nc.vector.reciprocal(inverse[:], scales[:]).then_inc(scale_step, 1)
            dve.wait_ge(scale_step, 4)
            nc.vector.scalar_tensor_tensor(out=checked[:], in0=inverse[:], scalar=0.0, in1=scales[:],
                                           op0=ALU.mult, op1=ALU.add).then_inc(scale_step, 1)
            dve.wait_ge(scale_step, 5)
            nc.vector.tensor_tensor(out_scale[:], checked[:, 1:2], checked[:, 2:3], ALU.mult).then_inc(scale_step, 1)
            with dve.Fori(0, NG // 4) as i:
                for u in range(2):
                    sum_and_add(i * 2 + u + 2, u)
                    lo_of_c(i * 2 + u, u)
            ternary(0, w1_sb, w1_t, 2, 0)
            sum_and_add(NG - 2, 0)
            ternary(1, w3_sb, w3_t, 4, 1)
            sum_and_add(NG - 1, 1)
            lo_of_c(NG - 4, 0)
            lo_of_c(NG - 3, 1)
            ternary(2, w2_sb, w2_t, 5, 2)
            lo_of_c(NG - 2, 0)
            lo_of_c(NG - 1, 1)

            def g_step(g, j):
                n, r = g * STEPS + j, rows_of(j)
                dve.wait_ge(silu_done, n + 1)
                if not (isinstance(g, int) and n < 3):
                    dve.wait_ge(g_lo_done, n - 2)
                if j < HC:
                    dve.wait_ge(h3_done, g * HC + j + 1)
                nc.vector.tensor_tensor(gf[j % 3][r], silu[j % 2][r], h3_of(j)[r] if j < HC else h1[j % 3][HR2:RM, :], ALU.mult
                                        ).then_inc(g_done, 1)

            def lo_step(g, j):
                dve.wait_ge(g_hi_done, g * STEPS + j + 1)
                hi = g_hi[j][:] if j < HC else g_rest[0:HR, :]
                lo = g_lo[j][:] if j < HC else g_rest[HR2:RM, :]
                nc.vector.tensor_tensor(lo, gf[j % 3][rows_of(j)], hi.bitcast(F32), ALU.subtract).then_inc(g_lo_done, 1)

            def residual(g):
                dve.wait_ge(got_xo, 16 * NG)
                for b in range(TT // 2):
                    dve.wait_ge(o_done[b], g + 1)
                    xg = xo[:, at(g), 2 * b:2 * b + 2, :]
                    xg = xg if isinstance(g, int) else xg.rearrange("p a t d -> p (a t) d")
                    nc.vector.scalar_tensor_tensor(out=xg, in0=o[b], scalar=out_scale[:, 0:1], in1=xg,
                                                   op0=ALU.mult, op1=ALU.add).then_inc(o_read[b], 1)

            g_step(0, 0)
            g_step(0, 1)
            lo_step(0, 0)
            with dve.Fori(0, NG - 1) as g:
                for j in range(STEPS):
                    g_step(*later(g, j, 2))
                    lo_step(*later(g, j, 1))
                residual(g)
            for j in range(STEPS):
                if j + 2 < STEPS:
                    g_step(NG - 1, j + 2)
                if j + 1 < STEPS:
                    lo_step(NG - 1, j + 1)
            residual(NG - 1)


_INS = ["x", "cond_1024", "L0_cond_W3", "L0_cond_b3", "L0_cond_W2", "L0_cond_b2", "L0_ffn_w1", "L0_ffn_w3", "L0_ffn_w2"]
_OUTS = [((128, 32, 256), "float32")]


def kernel(**inputs):
    import numpy as _np
    import concourse.bacc as _bacc
    from concourse import mybir as _mybir
    from concourse.bass_utils import run_bass_kernel_spmd as _run

    nc = _bacc.Bacc("TRN2", target_bir_lowering=False, num_devices=1)
    arrays, args = {}, []
    for name in _INS:
        a = _np.ascontiguousarray(inputs[name])
        arrays[f"in_{name}_dram"] = a
        args.append(nc.dram_tensor(f"in_{name}_dram", a.shape, _mybir.dt.from_np(a.dtype), kind="ExternalInput").ap())
    for i, (shape, dtype) in enumerate(_OUTS):
        dt = _mybir.dt.from_np(_np.dtype(dtype))
        args.append(nc.dram_tensor(f"out_{i}_dram", shape, dt, kind="ExternalOutput").ap())
    adaln_ternary_ffn_kernel(nc, *args)
    r = _run(nc, [arrays], core_ids=[0])
    return r.results[0]["out_0_dram"]
```

```python
from contextlib import ExitStack

import concourse.bass as bass
from concourse import mybir

F32 = mybir.dt.float32
F32R = mybir.dt.float32r
BF16 = mybir.dt.bfloat16
ALU = mybir.AluOpType
ACT = mybir.ActivationFunctionType
AX = mybir.AxisListType

P = 128
BANK = 512


def adaln_ternary_ffn_kernel(nc, x, cond, W3, b3, W2, b2, w1, w3, w2, out):
    B, S, D = x.shape
    Q = cond.shape[1]
    H = w1.shape[0]
    DC = D // P
    HC = H // P
    HR = H - HC * P
    HR2 = 64
    RM = HR2 + HR
    STEPS = HC + 1
    GT = BANK
    NG = B * S // GT
    GB = GT // S
    TT = GT // P
    W_COUNT = float(H * D)
    assert B == P and Q == P and HR <= 32 + 10 and 2 * HR <= P and NG == 8 and GT % S == 0

    x_v = x.rearrange("b s d -> (b s) d").rearrange("(g t p) d -> g p t d", t=TT, p=P)
    out_v = out.rearrange("b s d -> (b s) d").rearrange("(g t p) d -> g p t d", t=TT, p=P)

    with ExitStack() as ctx:
        def sb(name, shape, dt):
            return ctx.enter_context(nc.sbuf_tensor(name, shape, dt))

        def sem(name):
            return ctx.enter_context(nc.semaphore(name))

        cond_sb = sb("cond_sb", [P, Q], F32)
        b_rows = sb("b_rows", [2 * DC, P], F32)
        condT_b = sb("condT_b", [P, B + 2 * DC], F32)
        condT = condT_b[:, 0:B]
        b3_col = [condT_b[:, B + c:B + c + 1] for c in range(DC)]
        b2_col = [condT_b[:, B + DC + c:B + DC + c + 1] for c in range(DC)]
        W3_sb = sb("W3_sb", [P, D], F32)
        W2_sb = sb("W2_sb", [P, DC, D], F32)
        qT = sb("qT", [P, NG, DC, GB], F32)
        w1_sb = sb("w1_sb", [P, STEPS, D], F32)
        w3_sb = sb("w3_sb", [P, STEPS, D], F32)
        w2_sb = sb("w2_sb", [P, DC, H], F32)
        w1_t = sb("w1_t", [P, STEPS, D], BF16)
        w3_t = sb("w3_t", [P, STEPS, D], BF16)
        w2_t = sb("w2_t", [P, DC, H], BF16)
        below = sb("below", [P, STEPS * D], BF16)
        abs_sums = sb("abs_sums", [P, 6], F32)
        scales = sb("scales", [P, 3], F32)
        limits = sb("limits", [P, 3], F32)
        neg_limits = sb("neg_limits", [P, 3], F32)
        inverse = sb("inverse", [P, 3], F32)
        checked = sb("checked", [P, 3], F32)
        out_scale = sb("out_scale", [P, 1], F32)
        T13 = sb("T13", [P, DC, 2 * HC * P + P], F32R)
        T2 = sb("T2", [P, STEPS, D], F32R)
        ident = sb("ident", [P, P], F32)
        ident16 = sb("ident16", [P, P], BF16)
        ones = sb("ones", [P, P], F32)
        xs = [sb(f"xs{u}", [P, TT, D], F32) for u in range(2)]
        vsum = [sb(f"vsum{u}", [P, DC, GB], F32) for u in range(2)]
        y = [sb(f"y{u}", [P, DC, GT], F32) for u in range(2)]
        x1 = [sb(f"x1{u}", [P, DC, GT], F32) for u in range(2)]
        ct = [sb(f"ct{u}", [P, DC, GT], F32) for u in range(2)]
        c_hi = sb("c_hi", [P, NG, DC, GT], F32R)
        c_lo = sb("c_lo", [P, NG, DC, GT], F32R)
        silu = [y[u][:, 0, :] for u in range(2)]
        gf = [y[0][:, 1, :], y[1][:, 1, :], x1[0][:, 0, :]]
        g_hi = [sb(f"g_hi{j}", [P, GT], F32R) for j in range(HC)]
        g_lo = [sb(f"g_lo{j}", [P, GT], F32R) for j in range(HC)]
        g_rest = sb("g_rest", [P, GT], F32R)
        xo = sb("xo", [P, NG, TT, D], F32)

        bank = ctx.enter_context(nc.psum_tensor("bank", [P, 8, BANK], F32))
        xT = [bank[:, 2 * u:2 * u + DC, :] for u in range(2)]
        z = [bank[:, 4 + c, :] for c in range(DC)]
        h1 = [bank[:, 2 * s, :] for s in range(3)]
        h3 = [bank[:, 2 * s + 1, :] for s in range(3)]
        o = [bank[:, 6 + b, :].rearrange("p (t d) -> p t d", t=2) for b in range(TT // 2)]
        condT_b_ps = bank[:, 4, 0:B + 2 * DC]
        qT_ps = bank[:, 5, 0:DC * B].rearrange("p (c b) -> p c b", c=DC)
        sums_ps = bank[:, 6, 0:6]
        w_ps = [bank[:, 6 + b, :].bitcast(BF16) for b in range(2)]

        got_cond, got_W3, got_W2, got_b = sem("got_cond"), sem("got_W3"), sem("got_W2"), sem("got_b")
        got_w1, got_w3, got_w2 = sem("got_w1"), sem("got_w3"), sem("got_w2")
        got_xs = [sem(f"got_xs{u}") for u in range(2)]
        got_xo = sem("got_xo")
        stored = sem("stored")
        const_ready = sem("const_ready")
        zero_freey = sem("zero_freey")
        condT_done, condT_copied, q_done, q_ready = (sem("condT_done"), sem("condT_copied"), sem("q_done"),
                                                     sem("q_ready"))
        w1_abs_done, abs_done = sem("w1_abs_done"), sem("abs_done")
        sums_done, scale_step = sem("sums_done"), sem("scale_step")
        below_done, ternary_done = sem("below_done"), sem("ternary_done")
        wT_done, wT_copied = sem("wT_done"), sem("wT_copied")
        xT_done = sem("xT_done")
        vsum_done = sem("vsum_done")
        y_done = sem("y_done")
        x1_done = sem("x1_done")
        z_done = sem("z_done")
        z_free = [sem(f"z_free{c}") for c in range(DC)]
        c_hi_done = sem("c_hi_done")
        ct_free = sem("ct_free")
        late_lo_done = sem("late_lo_done")
        h1_done, h3_done = sem("h1_done"), sem("h3_done")
        silu_done, g_done, g_hi_done, g_lo_done = sem("silu_done"), sem("g_done"), sem("g_hi_done"), sem("g_lo_done")
        o_done = [sem(f"o_done{b}") for b in range(2)]
        o_free = [sem(f"o_free{b}") for b in range(2)]

        block = ctx.enter_context(nc.Block())

        def by_batch(ap):
            return ap.rearrange("p (b s) -> p b s", s=S)

        def over_sequence(ap):
            return ap.unsqueeze(2).broadcast_to([P, GB, S])

        def at(g):
            return g if isinstance(g, int) else bass.ds(g, 1)

        def group_of(tensor, g):
            return tensor[:, g] if isinstance(g, int) else \
                tensor[:, bass.ds(g, 1)].rearrange("p a c n -> p (a c) n")

        def rows_of(j):
            return slice(0, P) if j < HC else slice(0, HR)

        def later(g, j, by):
            return (g, j + by) if j + by < STEPS else (g + 1, j + by - STEPS)

        def output_after(j):
            return {0: (), 1: (0, 1)}.get(j, (j,))

        def h3_of(j):
            return h3[j % 3]

        @block.sync
        def _(sp):
            sp.sem_inc(ct_free, 2)
            for free in (*z_free, *o_free):
                sp.sem_inc(free, 1)
            sp.dma_start(cond_sb[:], cond).then_inc(got_cond, 16)
            sp.dma_start(xs[0][:], x_v[0]).then_inc(got_xs[0], 16)
            sp.dma_start(W3_sb[:], W3).then_inc(got_W3, 16)
            sp.dma_start(W2_sb[:], W2.rearrange("(c p) n -> p c n", p=P)).then_inc(got_W2, 16)
            sp.dma_start(xs[1][:], x_v[1]).then_inc(got_xs[1], 16)
            for u, w_sb, w, got in ((0, w1_sb, w1, got_w1), (1, w3_sb, w3, got_w3)):
                sp.dma_start(w_sb[:, 0:HC, :], w[0:HC * P, :].rearrange("(j p) d -> p j d", p=P)).then_inc(got, 16)
                sp.dma_start(w_sb[0:HR, HC, :], w[HC * P:H, :]).then_inc(got, 16)
                sp.wait_ge(xT_done, (u + 1) * DC)
                sp.dma_start(xs[u][:], x_v[u + 2]).then_inc(got_xs[u], 16)
            sp.dma_start(w2_sb[:], w2.rearrange("(c p) h -> p c h", p=P)).then_inc(got_w2, 16)
            with sp.Fori(1, NG // 2 - 1) as i:
                for u in range(2):
                    sp.wait_ge(xT_done, (i * 2 + u + 1) * DC)
                    sp.dma_start(xs[u][:], x_v[bass.ds(i * 2 + u + 2, 1)].rearrange("a p t d -> p (a t) d")
                                 ).then_inc(got_xs[u], 16)
            sp.dma_start(xo[:], x_v.rearrange("g p t d -> p g t d")).then_inc(got_xo, 16)
            with sp.Fori(0, NG) as g:
                for b in range(TT // 2):
                    sp.wait_ge(o_free[b], g + 2)
                    sp.dma_start(out_v[bass.ds(g, 1), :, 2 * b:2 * b + 2].rearrange("a p t d -> p (a t) d"),
                                 xo[:, bass.ds(g, 1), 2 * b:2 * b + 2].rearrange("p a t d -> p (a t) d")
                                 ).then_inc(stored, 16)
            sp.wait_ge(stored, 16 * NG * (TT // 2))

        @block.gpsimd
        def _(pool):
            nc.gpsimd.memset(ident[:], 0.0).then_inc(const_ready, 1)
            pool.wait_ge(const_ready, 1)
            nc.gpsimd.affine_select(out=ident[:], in_=ident[:], compare_op=ALU.not_equal, fill=1.0, base=0,
                                    pattern=[[-1, P]], channel_multiplier=1).then_inc(const_ready, 1)
            pool.wait_ge(const_ready, 2)
            nc.gpsimd.tensor_copy(ident16[:], ident[:]).then_inc(const_ready, 1)
            nc.gpsimd.memset(ones[:], 1.0).then_inc(const_ready, 1)
            nc.gpsimd.memset(abs_sums[:], 0.0).then_inc(zero_freey, 1)
            nc.gpsimd.memset(T13[:, :, 2 * HC * P:].bitcast(F32), 0.0).then_inc(zero_freey, 1)
            nc.gpsimd.memset(T2[:, HC, :].bitcast(F32), 0.0).then_inc(zero_freey, 1)
            nc.gpsimd.memset(g_rest[:].bitcast(F32), 0.0).then_inc(zero_freey, 1)

            def scale_by_q(g, u):
                for c in range(DC):
                    pool.wait_ge(y_done, g * DC + c + 1)
                    nc.gpsimd.tensor_tensor(by_batch(x1[u][:, c, :]), by_batch(y[u][:, c, :]),
                                            over_sequence(group_of(qT, g)[:, c, :]), ALU.mult).then_inc(x1_done, 1)

            pool.wait_ge(q_ready, DC)
            for g in range(2):
                scale_by_q(g, g)
            with pool.Fori(1, NG // 2 - 1) as i:
                for u in range(2):
                    pool.wait_ge(z_done, (i * 2 + u - 1) * DC)
                    scale_by_q(i * 2 + u, u)

            def lo_of_c(g, u):
                pool.wait_ge(c_hi_done, g + 1)
                nc.gpsimd.tensor_tensor(c_lo[:, g], ct[u][:], c_hi[:, g].bitcast(F32), ALU.subtract
                                        ).then_inc(late_lo_done, 1)

            for g in range(NG // 2, NG):
                if g + 2 < NG:
                    pool.wait_ge(z_done, (g + 1) * DC)
                    scale_by_q(g + 2, g % 2)
                lo_of_c(g, g % 2)

        @block.scalar
        def _(act):
            act.dma_start(b_rows[0:DC, :], b3.rearrange("(c p) -> c p", p=P)).then_inc(got_b, 16)
            act.dma_start(b_rows[DC:2 * DC, :], b2.rearrange("(c p) -> c p", p=P)).then_inc(got_b, 16)
            act.wait_ge(const_ready, 2)
            nc.scalar.activation(below[:, 0:1], ident[:, 0:1], ACT.Silu)
            act.wait_ge(condT_done, 1)
            nc.scalar.copy(condT_b[:], condT_b_ps).then_inc(condT_copied, 1)
            act.wait_ge(q_done, DC)
            for c in range(DC):
                nc.scalar.activation(qT[:, :, c, :], qT_ps[:, c, :].rearrange("p (g b) -> p g b", b=GB), ACT.Relu,
                                     bias=b3_col[c]).then_inc(q_ready, 1)
            def relu_and_hi(g, u):
                if isinstance(g, int) and g >= NG // 2 + 2:
                    act.wait_ge(late_lo_done, g - NG // 2 - 1)
                else:
                    act.wait_ge(ct_free, g + 1)
                for c in range(DC):
                    act.wait_ge(z_done, g * DC + c + 1)
                    nc.scalar.activation(ct[u][:, c, :], z[c], ACT.Relu, bias=b2_col[c]).then_inc(z_free[c], 1)
                act.wait_ge(z_free[DC - 1], g + 2)
                nc.scalar.copy(group_of(c_hi, g), ct[u][:]).then_inc(c_hi_done, 1)

            with act.Fori(0, NG // 4) as i:
                for u in range(2):
                    relu_and_hi(i * 2 + u, u)
            act.wait_ge(got_w3, 32)
            w3_rest = w3_sb[0:HR, HC, :]
            nc.scalar.activation(below[:, 0:HC * D], w3_sb[:, 0:HC, :].rearrange("p j d -> p (j d)"), ACT.Abs,
                                 accum_out=abs_sums[:, 2:3]).then_inc(abs_done, 1)
            nc.scalar.activation(below[0:HR, HC * D:], w3_rest, ACT.Abs, accum_out=abs_sums[0:HR, 3:4]
                                 ).then_inc(abs_done, 1)
            act.wait_ge(got_w2, 16)
            nc.scalar.activation(w2_t[:].rearrange("p c h -> p (c h)"), w2_sb[:].rearrange("p c h -> p (c h)"),
                                 ACT.Abs, accum_out=abs_sums[:, 4:5]).then_inc(abs_done, 1)
            for g in range(NG // 2, NG - 2):
                relu_and_hi(g, g % 2)
            act.wait_ge(zero_freey, 4)
            for k in range(2):
                act.wait_ge(wT_done, k + 1)
                for c in range(DC):
                    nc.scalar.copy(T13[:, c, k * HC * P:(k + 1) * HC * P], w_ps[c][:, 0:HC * P])
                    nc.scalar.copy(T13[:, c, 2 * HC * P + k * HR2:2 * HC * P + k * HR2 + HR],
                                   w_ps[c][:, HC * P:H]).then_inc(wT_copied, 1)
                relu_and_hi(NG - 2 + k, k)
            act.wait_ge(wT_done, 3)
            half = STEPS // 2
            nc.scalar.copy(T2[:, 0:half, :], w_ps[0][:, 0:half * D].rearrange("p (j d) -> p j d", d=D)
                           ).then_inc(wT_copied, 1)
            nc.scalar.copy(T2[:, half:HC, :], w_ps[1][:, 0:(HC - half) * D].rearrange("p (j d) -> p j d", d=D)
                           ).then_inc(wT_copied, 1)
            for row in (0, HR2):
                nc.scalar.copy(T2[row:row + HR, HC, :], w_ps[1][0:HR, (HC - half) * D:STEPS * D - half * D]
                               ).then_inc(wT_copied, 1)

            def silu_step(g, j):
                r = rows_of(j)
                act.wait_ge(h1_done, g * STEPS + j + 1)
                nc.scalar.activation(silu[j % 2][r], h1[j % 3][r], ACT.Silu, scale=checked[r, 0:1]
                                     ).then_inc(silu_done, 1)

            def hi_step(g, j):
                act.wait_ge(g_done, g * STEPS + j + 1)
                nc.scalar.copy(g_hi[j][:] if j < HC else g_rest[0:HR, :], gf[j % 3][rows_of(j)]).then_inc(g_hi_done, 1)

            act.wait_ge(scale_step, 8)
            silu_step(0, 0)
            with act.Fori(0, NG - 1) as g:
                for j in range(STEPS):
                    silu_step(*later(g, j, 1))
                    hi_step(g, j)
            for j in range(STEPS):
                if j + 1 < STEPS:
                    silu_step(NG - 1, j + 1)
                hi_step(NG - 1, j)

        @block.tensor
        def _(pe):
            pe.wait_ge(got_cond, 16)
            pe.wait_ge(const_ready, 4)
            pe.transpose(condT_b_ps[:, 0:B], cond_sb[:], ident[:])
            pe.wait_ge(got_b, 16 * 2)
            pe.transpose(condT_b_ps[:, B:B + 2 * DC], b_rows[:], ident[0:2 * DC, 0:2 * DC]).then_inc(condT_done, 1)
            pe.wait_ge(got_W3, 16)
            pe.wait_ge(condT_copied, 1)
            for c in range(DC):
                pe.matmul(qT_ps[:, c, :], W3_sb[:, c * P:(c + 1) * P], condT, start=True, stop=True
                          ).then_inc(q_done, 1)

            def transpose_x(u, load):
                pe.wait_ge(got_xs[u], load * 16 + 16)
                for c in range(DC):
                    for t in range(TT):
                        last = pe.transpose(xT[u][:, c, t * P:(t + 1) * P], xs[u][:, t, c * P:(c + 1) * P], ident[:])
                    last.then_inc(xT_done, 1)

            def project_c(g, u, c):
                pe.wait_ge(z_free[c], g + 1)
                for k in range(DC):
                    if c == 0:
                        pe.wait_ge(x1_done, g * DC + k + 1)
                    last = pe.matmul(z[c], W2_sb[:, k, c * P:(c + 1) * P], x1[u][:, k, :],
                                     start=(k == 0), stop=(k == DC - 1))
                last.then_inc(z_done, 1)

            transpose_x(0, 0)
            transpose_x(1, 0)
            pe.wait_ge(got_W2, 16)
            pe.wait_ge(q_ready, DC)
            with pe.Fori(0, NG // 4) as i:
                for u in range(2):
                    project_c(i * 2 + u, u, 0)
                    pe.wait_ge(y_done, (i * 2 + u + 1) * DC)
                    transpose_x(u, i + 1)
                    project_c(i * 2 + u, u, 1)

            def sum_partitions(col, n, done):
                pe.wait_ge(done, 2 if done is w1_abs_done else 3)
                pe.matmul(sums_ps[:, col:col + n], ones[:], abs_sums[:, col:col + n], start=True, stop=True
                          ).then_inc(sums_done, 1)

            sum_partitions(0, 2, w1_abs_done)
            for g in range(NG // 2, NG - 2):
                project_c(g, g % 2, 0)
                pe.wait_ge(y_done, (g + 1) * DC)
                transpose_x(g % 2, g // 2 + 1)
                project_c(g, g % 2, 1)
                if g == NG // 2:
                    pe.wait_ge(scale_step, 1)
                    sum_partitions(2, 3, abs_done)

            def transpose_w(k, w_t):
                pe.wait_ge(ternary_done, k + 1)
                for c in range(DC):
                    pe.wait_ge(scale_step, 4) if k == 0 else pe.wait_ge(wT_copied, c + 1)
                    for j in range(STEPS):
                        rows = P if j < HC else HR
                        last = pe.transpose(w_ps[c][:, j * P:j * P + rows], w_t[0:rows, j, c * P:(c + 1) * P],
                                            ident16[0:rows, 0:rows])
                last.then_inc(wT_done, 1)

            transpose_w(0, w1_t)
            project_c(NG - 2, 0, 0)
            project_c(NG - 2, 0, 1)
            transpose_w(1, w3_t)
            project_c(NG - 1, 1, 0)
            project_c(NG - 1, 1, 1)
            def hidden_step(g, j):
                w = P if j < HC else RM
                products = [(h1, j * P, h1_done), (h3, (HC + j) * P, h3_done)] if j < HC else \
                    [(h1, 2 * HC * P, h1_done)]
                passes = [(k, part) for k in range(DC) for part in (c_hi, c_lo)]
                for dst, col, done in products:
                    for i, (k, part) in enumerate(passes):
                        moving = part[:, at(g), k, :]
                        last = pe.matmul(dst[j % 3][0:w, :], T13[:, k, col:col + w], moving,
                                         start=(i == 0), stop=(i == len(passes) - 1))
                    last.then_inc(done, 1)

            def output_step(g, j):
                pe.wait_ge(g_lo_done, g * STEPS + j + 1)
                parts = [(g_hi[j], P), (g_lo[j], P)] if j < HC else [(g_rest, RM)]
                for b in range(TT // 2):
                    if j == 0:
                        pe.wait_ge(o_free[b], g + 1)
                    for i, (part, rows) in enumerate(parts):
                        for t in range(2):
                            col = (2 * b + t) * P
                            last = pe.matmul(o[b][:, t, :], part[0:rows, col:col + P], T2[0:rows, j, :],
                                             start=(j == 0 and i == 0 and t == 0), stop=(j == HC),
                                             skip_group_check=True)
                    if j == HC:
                        last.then_inc(o_done[b], 1)

            pe.wait_ge(wT_copied, 2 * DC)
            pe.wait_ge(ct_free, 2 + NG // 2)
            pe.wait_ge(y_done, NG * DC)
            hidden_step(0, 0)
            hidden_step(0, 1)
            pe.wait_ge(ternary_done, 3)
            half = STEPS // 2
            for j in range(STEPS):
                rows = P if j < HC else HR
                for c in range(DC):
                    col = (j % half) * D + c * P
                    last = pe.transpose(w_ps[j // half][0:rows, col:col + P], w2_t[:, c, j * P:j * P + rows], ident16[:])
            last.then_inc(wT_done, 1)
            for c in range(DC):
                pe.wait_ge(z_free[c], NG + 1)
            pe.wait_ge(late_lo_done, NG // 2)
            hidden_step(0, 2)
            pe.wait_ge(wT_copied, 2 * DC + 4)
            with pe.Fori(0, NG - 1) as g:
                for j in range(STEPS):
                    pe.wait_ge(g_done, g * STEPS + j + 1)
                    hidden_step(*later(g, j, 3))
                    for done in output_after(j):
                        output_step(g, done)
            for j in range(STEPS):
                if j + 3 < STEPS:
                    pe.wait_ge(g_done, (NG - 1) * STEPS + j + 1)
                    hidden_step(NG - 1, j + 3)
                for done in output_after(j):
                    output_step(NG - 1, done)

        @block.vector
        def _(dve):
            def sum_and_add(g, u):
                for c in range(DC):
                    dve.wait_ge(xT_done, g * DC + c + 1)
                    nc.vector.tensor_reduce(vsum[u][:, c, :], by_batch(xT[u][:, c, :]), AX.X, ALU.add
                                            ).then_inc(vsum_done, 1)
                for c in range(DC):
                    dve.wait_ge(vsum_done, g * DC + c + 1)
                    nc.vector.scalar_tensor_tensor(
                        out=by_batch(y[u][:, c, :]), in0=by_batch(xT[u][:, c, :]), scalar=float(S),
                        in1=over_sequence(vsum[u][:, c, :]), op0=ALU.mult, op1=ALU.add).then_inc(y_done, 1)

            def lo_of_c(g, u):
                dve.wait_ge(c_hi_done, g + 1)
                nc.vector.tensor_tensor(group_of(c_lo, g), ct[u][:], group_of(c_hi, g).bitcast(F32), ALU.subtract
                                        ).then_inc(ct_free, 1)

            def ternary(k, w_sb, w_t, n, col):
                w, t = (a[:].rearrange("p a b -> p (a b)") for a in (w_sb, w_t))
                rows = [(0, P, 0, HC * D), (0, HR, HC * D, STEPS * D)] if k < 2 else [(0, P, 0, DC * H)]
                if k:
                    dve.wait_ge(ternary_done, k)
                for r0, r1, a, b in rows:
                    nc.vector.tensor_scalar(below[r0:r1, a:b], w[r0:r1, a:b], neg_limits[r0:r1, col:col + 1], None,
                                            ALU.is_lt).then_inc(below_done, 1)
                dve.wait_ge(below_done, n)
                for i, (r0, r1, a, b) in enumerate(rows):
                    last = nc.vector.scalar_tensor_tensor(
                        out=t[r0:r1, a:b], in0=w[r0:r1, a:b], scalar=limits[r0:r1, col:col + 1],
                        in1=below[r0:r1, a:b], op0=ALU.is_gt, op1=ALU.subtract)
                last.then_inc(ternary_done, 1)

            sum_and_add(0, 0)
            sum_and_add(1, 1)
            dve.wait_ge(got_w1, 32)
            dve.wait_ge(zero_freey, 1)
            for rows, chunks, col in ((P, slice(0, HC), 0), (HR, slice(HC, STEPS), 1)):
                nc.vector.tensor_reduce(abs_sums[0:rows, col:col + 1], w1_sb[0:rows, chunks, :], AX.XY, ALU.add,
                                        apply_absolute_value=True).then_inc(w1_abs_done, 1)
            with dve.Fori(0, NG // 4) as i:
                for u in range(2):
                    sum_and_add(i * 2 + u + 2, u)
                    lo_of_c(i * 2 + u, u)

            def scale_and_limits(n, col, sums):
                nc.vector.tensor_copy(abs_sums[:, 2 * col:2 * col + sums], sums_ps[:, 2 * col:2 * col + sums]
                                      ).then_inc(scale_step, 1)
                dve.wait_ge(scale_step, n + 1)
                cols = range(col, col + (sums + 1) // 2)
                for k in cols:
                    second = abs_sums[:, 2 * k + 1:2 * k + 2] if 2 * k + 1 < 2 * col + sums else 0.0
                    last = nc.vector.tensor_scalar(scales[:, k:k + 1], abs_sums[:, 2 * k:2 * k + 1], second,
                                                   1.0 / W_COUNT, ALU.add, ALU.mult)
                last.then_inc(scale_step, 1)
                dve.wait_ge(scale_step, n + 2)
                own = slice(col, cols[-1] + 1)
                nc.vector.tensor_scalar(limits[:, own], scales[:, own], 0.5, None, ALU.mult)
                nc.vector.tensor_scalar(neg_limits[:, own], scales[:, own], -0.5, None, ALU.mult
                                        ).then_inc(scale_step, 1)
                dve.wait_ge(scale_step, n + 3)

            dve.wait_ge(sums_done, 1)
            scale_and_limits(0, 0, 2)
            sum_and_add(NG - 2, 0)
            dve.wait_ge(abs_done, 2)
            ternary(0, w1_sb, w1_t, 2, 0)
            dve.wait_ge(sums_done, 2)
            scale_and_limits(3, 1, 3)
            sum_and_add(NG - 1, 1)
            ternary(1, w3_sb, w3_t, 4, 1)
            ternary(2, w2_sb, w2_t, 5, 2)
            nc.vector.reciprocal(inverse[:], scales[:]).then_inc(scale_step, 1)
            dve.wait_ge(scale_step, 7)
            nc.vector.scalar_tensor_tensor(out=checked[:], in0=inverse[:], scalar=0.0, in1=scales[:],
                                           op0=ALU.mult, op1=ALU.add).then_inc(scale_step, 1)
            dve.wait_ge(scale_step, 8)
            nc.vector.tensor_tensor(out_scale[:], checked[:, 1:2], checked[:, 2:3], ALU.mult).then_inc(scale_step, 1)
            dve.wait_ge(scale_step, 9)

            def g_step(g, j):
                n, r = g * STEPS + j, rows_of(j)
                dve.wait_ge(silu_done, n + 1)
                if not (isinstance(g, int) and g == 0 and j < 3):
                    dve.wait_ge(g_lo_done, n - 2)
                if j < HC:
                    dve.wait_ge(h3_done, g * HC + j + 1)
                nc.vector.tensor_tensor(gf[j % 3][r], silu[j % 2][r], h3_of(j)[r] if j < HC else h1[j % 3][HR2:RM, :], ALU.mult
                                        ).then_inc(g_done, 1)

            def lo_step(g, j):
                dve.wait_ge(g_hi_done, g * STEPS + j + 1)
                hi = g_hi[j][:] if j < HC else g_rest[0:HR, :]
                lo = g_lo[j][:] if j < HC else g_rest[HR2:RM, :]
                nc.vector.tensor_tensor(lo, gf[j % 3][rows_of(j)], hi.bitcast(F32), ALU.subtract).then_inc(g_lo_done, 1)

            def residual(g, b):
                dve.wait_ge(o_done[b], g + 1)
                xg = xo[:, at(g), 2 * b:2 * b + 2, :]
                xg = xg if isinstance(g, int) else xg.rearrange("p a t d -> p (a t) d")
                nc.vector.scalar_tensor_tensor(out=xg, in0=o[b], scalar=out_scale[:, 0:1], in1=xg,
                                               op0=ALU.mult, op1=ALU.add).then_inc(o_free[b], 1)

            dve.wait_ge(got_xo, 16)
            g_step(0, 0)
            for j in range(2):
                g_step(0, j + 1)
                lo_step(0, j)
            with dve.Fori(0, NG - 1) as g:
                for j in range(STEPS):
                    g_step(*later(g, j, 3))
                    lo_step(*later(g, j, 2))
                for b in range(TT // 2):
                    residual(g, b)
            for j in range(STEPS):
                if j + 3 < STEPS:
                    g_step(NG - 1, j + 3)
                if j + 2 < STEPS:
                    lo_step(NG - 1, j + 2)
            for b in range(TT // 2):
                residual(NG - 1, b)


_INS = ["x", "cond_1024", "L0_cond_W3", "L0_cond_b3", "L0_cond_W2", "L0_cond_b2", "L0_ffn_w1", "L0_ffn_w3", "L0_ffn_w2"]
_OUTS = [((128, 32, 256), "float32")]


def kernel(**inputs):
    import numpy as _np
    import concourse.bacc as _bacc
    from concourse import mybir as _mybir
    from concourse.bass_utils import run_bass_kernel_spmd as _run

    nc = _bacc.Bacc("TRN2", target_bir_lowering=False, num_devices=1)
    arrays, args = {}, []
    for name in _INS:
        a = _np.ascontiguousarray(inputs[name])
        arrays[f"in_{name}_dram"] = a
        args.append(nc.dram_tensor(f"in_{name}_dram", a.shape, _mybir.dt.from_np(a.dtype), kind="ExternalInput").ap())
    for i, (shape, dtype) in enumerate(_OUTS):
        dt = _mybir.dt.from_np(_np.dtype(dtype))
        args.append(nc.dram_tensor(f"out_{i}_dram", shape, dt, kind="ExternalOutput").ap())
    adaln_ternary_ffn_kernel(nc, *args)
    r = _run(nc, [arrays], core_ids=[0])
    return r.results[0]["out_0_dram"]
```

```python
from contextlib import ExitStack

import concourse.bass as bass
from concourse import mybir

F32 = mybir.dt.float32
F32R = mybir.dt.float32r
BF16 = mybir.dt.bfloat16
ALU = mybir.AluOpType
ACT = mybir.ActivationFunctionType
AX = mybir.AxisListType

P = 128
WARM_UP = 6
BANK = 512


def adaln_ternary_ffn_kernel(nc, x, cond, W3, b3, W2, b2, w1, w3, w2, out):
    B, S, D = x.shape
    Q = cond.shape[1]
    H = w1.shape[0]
    DC = D // P
    HC = H // P
    HR = H - HC * P
    HR2 = 64
    RM = HR2 + HR
    W2_HALF = (HC + 1) // 2
    STEPS = HC + 1
    GT = BANK
    NG = B * S // GT
    GB = GT // S
    TT = GT // P
    HALVES = 2
    HT = GT // HALVES
    HB = GB // HALVES
    HTT = TT // HALVES
    W_COUNT = float(H * D)
    assert B == P and Q == P and HR <= HR2 and RM <= P and NG == 8 and HT % S == 0 and DC == 2

    x_v = x.rearrange("b s d -> (b s) d").rearrange("(g t p) d -> g p t d", t=TT, p=P)
    out_v = out.rearrange("b s d -> (b s) d").rearrange("(g t p) d -> g p t d", t=TT, p=P)

    with ExitStack() as ctx:
        def sb(name, shape, dt):
            return ctx.enter_context(nc.sbuf_tensor(name, shape, dt))

        def sem(name):
            return ctx.enter_context(nc.semaphore(name))

        cond_sb = sb("cond_sb", [P, Q], F32)
        b_rows = sb("b_rows", [2 * DC, P], F32)
        condT_b = sb("condT_b", [P, B + 2 * DC], F32)
        condT = condT_b[:, 0:B]
        b3_col = [condT_b[:, B + c:B + c + 1] for c in range(DC)]
        b2_col = [condT_b[:, B + DC + c:B + DC + c + 1] for c in range(DC)]
        W3_sb = sb("W3_sb", [P, D], F32)
        W2_sb = sb("W2_sb", [P, DC, D], F32)
        qT = sb("qT", [P, NG * HALVES, DC, HB], F32)
        w1_sb = sb("w1_sb", [P, STEPS, D], F32)
        w3_sb = sb("w3_sb", [P, STEPS, D], F32)
        w2_sb = sb("w2_sb", [P, DC, H], F32)
        w1_t = sb("w1_t", [P, STEPS, D], BF16)
        w3_t = sb("w3_t", [P, STEPS, D], BF16)
        w2_t = sb("w2_t", [P, DC, H], BF16)
        below = sb("below", [P, STEPS * D], BF16)
        abs_sums = sb("abs_sums", [P, 5], F32)
        scales = sb("scales", [P, 3], F32)
        limits = sb("limits", [P, 3], F32)
        neg_limits = sb("neg_limits", [P, 3], F32)
        inverse = sb("inverse", [P, 3], F32)
        checked = sb("checked", [P, 3], F32)
        out_scale = sb("out_scale", [P, 1], F32)
        T13 = sb("T13", [P, DC, 2 * HC * P + P], F32R)
        T2 = sb("T2", [P, STEPS, D], F32R)
        ident = sb("ident", [P, P], F32)
        ident16 = sb("ident16", [P, P], BF16)
        ones = sb("ones", [P, P], F32)
        xs = [sb(f"xs{u}", [P, TT, D], F32) for u in range(2)]
        vsum = [sb(f"vsum{u}", [P, HALVES, DC * HB], F32) for u in range(2)]
        y = [sb(f"y{u}", [P, HALVES, DC, HT], F32) for u in range(2)]
        x1 = [sb(f"x1{u}", [P, HALVES, DC, HT], F32) for u in range(2)]
        ct = [sb(f"ct{u}", [P, DC, GT], F32) for u in range(2)]
        c_hi = sb("c_hi", [P, NG, DC, GT], F32R)
        c_lo = sb("c_lo", [P, NG, DC, GT], F32R)
        silu = [t.rearrange("p c n -> p (c n)") for t in (y[0][:, 0], y[1][:, 0])]
        gf = [t.rearrange("p c n -> p (c n)") for t in (y[0][:, 1], y[1][:, 1], x1[0][:, 0])]
        g_hi = [sb(f"g_hi{j}", [P, GT], F32R) for j in range(HC)]
        g_lo = [sb(f"g_lo{j}", [P, GT], F32R) for j in range(HC)]
        g_rest = sb("g_rest", [P, GT], F32R)
        xo = sb("xo", [P, NG, TT, D], F32)

        bank = ctx.enter_context(nc.psum_tensor("bank", [P, 8, BANK], F32))
        xT = [[bank[:, 2 * u + h, :] for h in range(HALVES)] for u in range(2)]
        z = [bank[:, 4 + c, :] for c in range(DC)]
        h1 = [bank[:, 2 * s, :] for s in range(3)]
        h3 = [bank[:, 2 * s + 1, :] for s in range(3)]
        o = [bank[:, 6 + b, :].rearrange("p (t d) -> p t d", t=2) for b in range(TT // 2)]
        o_last = bank[:, 5, 0:D]
        condT_b_ps = bank[:, 4, 0:B + 2 * DC]
        qT_ps = bank[:, 5, 0:DC * B].rearrange("p (c b) -> p c b", c=DC)
        sums_ps = [bank[:, 6, 0:1], bank[:, 7, 0:2]]
        w_ps = [bank[:, 6 + b, :].bitcast(BF16) for b in range(2)]

        got_cond, got_W3, got_W2, got_b = sem("got_cond"), sem("got_W3"), sem("got_W2"), sem("got_b")
        got_w1, got_w3, got_w2 = sem("got_w1"), sem("got_w3"), sem("got_w2")
        got_x0 = sem("got_x0")
        got_xs = [sem(f"got_xs{u}") for u in range(2)]
        got_xo = sem("got_xo")
        stored = sem("stored")
        const_ready = sem("const_ready")
        zeroed = sem("zeroed")
        condT_done, condT_copied, q_done, q_ready = (sem("condT_done"), sem("condT_copied"), sem("q_done"),
                                                     sem("q_ready"))
        w1_abs_done, abs_done = sem("w1_abs_done"), sem("abs_done")
        sums_done = sem("sums_done")
        scale_step = sem("scale_step")
        below_done, ternary_done = sem("below_done"), sem("ternary_done")
        wT_done = sem("wT_done")
        wT_copied, T2_copied = sem("wT_copied"), sem("T2_copied")
        xT_done = sem("xT_done")
        vsum_done = sem("vsum_done")
        y_done = sem("y_done")
        x1_done = sem("x1_done")
        z_done = sem("z_done")
        z_free = [sem(f"z_free{c}") for c in range(DC)]
        c_hi_done = sem("c_hi_done")
        ct_free = sem("ct_free")
        late_lo_done = sem("late_lo_done")
        h1_done, h3_done = sem("h1_done"), sem("h3_done")
        silu_done, g_done, g_hi_done, g_lo_done = sem("silu_done"), sem("g_done"), sem("g_hi_done"), sem("g_lo_done")
        o_done = [sem(f"o_done{b}") for b in range(2)]
        o_free = [sem(f"o_free{b}") for b in range(2)]

        block = ctx.enter_context(nc.Block())

        def by_batch(ap):
            return ap.rearrange("p (b s) -> p b s", s=S)

        def flat(ap):
            return ap.rearrange("p c n -> p (c n)")

        def over_sequence(ap):
            return ap.unsqueeze(2).broadcast_to([P, DC * HB, S])

        def at(g):
            return g if isinstance(g, int) else bass.ds(g, 1)

        def group_of(tensor, g):
            return tensor[:, g] if isinstance(g, int) else \
                tensor[:, bass.ds(g, 1)].rearrange("p a c n -> p (a c) n")

        def rows_of(j):
            return slice(0, P) if j < HC else slice(0, HR)

        def later(g, j, by):
            return (g, j + by) if j + by < STEPS else (g + 1, j + by - STEPS)

        def output_after(j):
            return {0: (), 1: (0, 1)}.get(j, (j,))

        @block.sync
        def _(sp):
            sp.sem_inc(ct_free, 2)
            for free in (*z_free, *o_free):
                sp.sem_inc(free, 1)
            sp.dma_start(xs[0][:, 0:HTT], x_v[0, :, 0:HTT]).then_inc(got_x0, 16)
            sp.dma_start(cond_sb[:], cond).then_inc(got_cond, 16)
            sp.dma_start(W3_sb[:], W3).then_inc(got_W3, 16)
            sp.dma_start(xs[0][:, HTT:TT], x_v[0, :, HTT:TT]).then_inc(got_xs[0], 16)
            sp.dma_start(xs[1][:], x_v[1]).then_inc(got_xs[1], 16)
            sp.dma_start(W2_sb[:], W2.rearrange("(c p) n -> p c n", p=P)).then_inc(got_W2, 16)
            for u, w_sb, w, got in ((0, w1_sb, w1, got_w1), (1, w3_sb, w3, got_w3)):
                sp.wait_ge(xT_done, (u + 1) * HALVES)
                sp.dma_start(xs[u][:], x_v[u + 2]).then_inc(got_xs[u], 16)
                sp.dma_start(w_sb[:, 0:HC, :], w[0:HC * P, :].rearrange("(j p) d -> p j d", p=P)).then_inc(got, 16)
                sp.dma_start(w_sb[0:HR, HC, :], w[HC * P:H, :]).then_inc(got, 16)
            sp.dma_start(w2_sb[:], w2.rearrange("(c p) h -> p c h", p=P)).then_inc(got_w2, 16)
            with sp.Fori(1, NG // 2 - 1) as i:
                for u in range(2):
                    sp.wait_ge(xT_done, (i * 2 + u + 1) * HALVES)
                    sp.dma_start(xs[u][:], x_v[bass.ds(i * 2 + u + 2, 1)].rearrange("a p t d -> p (a t) d")
                                 ).then_inc(got_xs[u], 16)
            sp.dma_start(xo[:], x_v.rearrange("g p t d -> p g t d")).then_inc(got_xo, 16)
            with sp.Fori(0, NG - 1) as g:
                for b in range(TT // 2):
                    sp.wait_ge(o_free[b], g + 2)
                    sp.dma_start(out_v[bass.ds(g, 1), :, 2 * b:2 * b + 2].rearrange("a p t d -> p (a t) d"),
                                 xo[:, bass.ds(g, 1), 2 * b:2 * b + 2].rearrange("p a t d -> p (a t) d")
                                 ).then_inc(stored, 16)
            for b, t0, t1, n in ((0, 0, 2, 1), (1, 2, 3, 1), (1, 3, 4, 2)):
                sp.wait_ge(o_free[b], NG + n)
                sp.dma_start(out_v[NG - 1, :, t0:t1], xo[:, NG - 1, t0:t1]).then_inc(stored, 16)
            sp.wait_ge(stored, 16 * (NG * (TT // 2) + 1))

        @block.gpsimd
        def _(pool):
            nc.gpsimd.memset(ident[:], 0.0).then_inc(const_ready, 1)
            pool.wait_ge(const_ready, 1)
            nc.gpsimd.affine_select(out=ident[:], in_=ident[:], compare_op=ALU.not_equal, fill=1.0, base=0,
                                    pattern=[[-1, P]], channel_multiplier=1).then_inc(const_ready, 1)
            pool.wait_ge(const_ready, 2)
            nc.gpsimd.tensor_copy(ident16[:], ident[:]).then_inc(const_ready, 1)
            nc.gpsimd.memset(ones[:], 1.0).then_inc(const_ready, 1)
            nc.gpsimd.memset(abs_sums[:], 0.0).then_inc(zeroed, 1)
            nc.gpsimd.memset(T13[:, :, 2 * HC * P:].bitcast(F32), 0.0).then_inc(zeroed, 1)
            nc.gpsimd.memset(T2[:, HC, :].bitcast(F32), 0.0).then_inc(zeroed, 1)
            nc.gpsimd.memset(g_rest[:].bitcast(F32), 0.0).then_inc(zeroed, 1)

            def scale_by_q(g, u):
                for h in range(HALVES):
                    pool.wait_ge(y_done, g * HALVES + h + 1)
                    gh = g * HALVES + h
                    q_half = qT[:, gh] if isinstance(g, int) else \
                        qT[:, bass.ds(gh, 1)].rearrange("p a c b -> p (a c) b")
                    nc.gpsimd.tensor_tensor(by_batch(flat(x1[u][:, h])), by_batch(flat(y[u][:, h])),
                                            over_sequence(flat(q_half)), ALU.mult).then_inc(x1_done, 1)

            pool.wait_ge(q_ready, DC)
            for g in range(2):
                scale_by_q(g, g)
            with pool.Fori(1, NG // 2 - 1) as i:
                for u in range(2):
                    pool.wait_ge(z_done, (i * 2 + u - 1) * DC)
                    scale_by_q(i * 2 + u, u)

            def lo_of_c(g, u):
                pool.wait_ge(c_hi_done, g + 1)
                nc.gpsimd.tensor_tensor(c_lo[:, g], ct[u][:], c_hi[:, g].bitcast(F32), ALU.subtract
                                        ).then_inc(late_lo_done, 1)

            for g in range(NG // 2, NG):
                if g + 2 < NG:
                    pool.wait_ge(z_done, (g + 1) * DC)
                    scale_by_q(g + 2, g % 2)
                lo_of_c(g, g % 2)

        @block.scalar
        def _(act):
            act.dma_start(b_rows[0:DC, :], b3.rearrange("(c p) -> c p", p=P)).then_inc(got_b, 16)
            act.dma_start(b_rows[DC:2 * DC, :], b2.rearrange("(c p) -> c p", p=P)).then_inc(got_b, 16)
            act.wait_ge(const_ready, 2)
            nc.scalar.activation(below[:, 0:1], ident[:, 0:1], ACT.Silu)
            act.wait_ge(condT_done, 1)
            nc.scalar.copy(condT_b[:], condT_b_ps).then_inc(condT_copied, 1)
            act.wait_ge(q_done, DC)
            for c in range(DC):
                nc.scalar.activation(qT[:, :, c, :], qT_ps[:, c, :].rearrange("p (h b) -> p h b", b=HB), ACT.Relu,
                                     bias=b3_col[c]).then_inc(q_ready, 1)

            def relu_and_hi(g, u):
                if isinstance(g, int) and g >= NG // 2 + 2:
                    act.wait_ge(late_lo_done, g - NG // 2 - 1)
                else:
                    act.wait_ge(ct_free, g + 1)
                for c in range(DC):
                    act.wait_ge(z_done, g * DC + c + 1)
                    nc.scalar.activation(ct[u][:, c, :], z[c], ACT.Relu, bias=b2_col[c]).then_inc(z_free[c], 1)
                act.wait_ge(z_free[DC - 1], g + 2)
                nc.scalar.copy(group_of(c_hi, g), ct[u][:]).then_inc(c_hi_done, 1)

            with act.Fori(0, NG // 4) as i:
                for u in range(2):
                    relu_and_hi(i * 2 + u, u)
            act.wait_ge(got_w3, 32)
            w3_rest = w3_sb[0:HR, HC, :]
            nc.scalar.activation(below[:, 0:HC * D], w3_sb[:, 0:HC, :].rearrange("p j d -> p (j d)"), ACT.Abs,
                                 accum_out=abs_sums[:, 1:2]).then_inc(abs_done, 1)
            nc.scalar.activation(below[0:HR, HC * D:], w3_rest, ACT.Abs, accum_out=abs_sums[0:HR, 4:5]
                                 ).then_inc(abs_done, 1)
            relu_and_hi(NG // 2, 0)
            act.wait_ge(got_w2, 16)
            nc.scalar.activation(w2_t[:].rearrange("p c h -> p (c h)"), w2_sb[:].rearrange("p c h -> p (c h)"),
                                 ACT.Abs, accum_out=abs_sums[:, 2:3]).then_inc(abs_done, 1)
            relu_and_hi(NG // 2 + 1, 1)

            def copy_T13(k):
                act.wait_ge(wT_done, k + 1)
                for c in range(DC):
                    nc.scalar.copy(T13[:, c, k * HC * P:(k + 1) * HC * P], w_ps[c][:, 0:HC * P])
                    nc.scalar.copy(T13[:, c, 2 * HC * P + k * HR2:2 * HC * P + k * HR2 + HR],
                                   w_ps[c][:, HC * P:H]).then_inc(wT_copied, 1)

            relu_and_hi(NG - 2, 0)
            act.wait_ge(zeroed, 4)
            copy_T13(0)
            copy_T13(1)
            relu_and_hi(NG - 1, 1)

            def silu_step(g, j):
                r = rows_of(j)
                act.wait_ge(h1_done, g * STEPS + j + 1)
                nc.scalar.activation(silu[j % 2][r], h1[j % 3][r], ACT.Silu, scale=checked[r, 0:1]
                                     ).then_inc(silu_done, 1)

            def hi_step(g, j):
                act.wait_ge(g_done, g * STEPS + j + 1)
                hi = g_hi[j][:] if j < HC else g_rest[0:HR, :]
                nc.scalar.copy(hi, gf[j % 3][rows_of(j)]).then_inc(g_hi_done, 1)

            act.wait_ge(scale_step, 4)
            silu_step(0, 0)
            act.wait_ge(wT_done, 3)
            nc.scalar.copy(T2[:, W2_HALF:HC, :], w_ps[1][:, 0:(HC - W2_HALF) * D].rearrange("p (j d) -> p j d", d=D)
                           ).then_inc(T2_copied, 1)
            for row in (0, HR2):
                nc.scalar.copy(T2[row:row + HR, HC, :], w_ps[1][0:HR, (HC - W2_HALF) * D:(STEPS - W2_HALF) * D]
                               ).then_inc(T2_copied, 1)
            with act.Fori(0, NG - 1) as g:
                for j in range(STEPS):
                    silu_step(*later(g, j, 1))
                    hi_step(g, j)
            for j in range(STEPS):
                if j + 1 < STEPS:
                    silu_step(NG - 1, j + 1)
                hi_step(NG - 1, j)

        @block.tensor
        def _(pe):
            def transpose_x(u, h):
                for c in range(DC):
                    for t in range(HTT):
                        col = c * HT + t * P
                        last = pe.transpose(xT[u][h][:, col:col + P], xs[u][:, h * HTT + t, c * P:(c + 1) * P],
                                            ident[:])
                last.then_inc(xT_done, 1)

            def project_c(g, u):
                for h in range(HALVES):
                    pe.wait_ge(x1_done, g * HALVES + h + 1)
                    for c in range(DC):
                        if h == 0:
                            pe.wait_ge(z_free[c], g + 1)
                        for k in range(DC):
                            last = pe.matmul(z[c][:, h * HT:(h + 1) * HT], W2_sb[:, k, c * P:(c + 1) * P],
                                             x1[u][:, h, k, :], start=(k == 0), stop=(k == DC - 1))
                        if h == HALVES - 1:
                            last.then_inc(z_done, 1)

            def transpose_next(g, u, load):
                pe.wait_ge(got_xs[u], load * 16 + 16)
                for h in range(HALVES):
                    pe.wait_ge(y_done, g * HALVES + h + 1)
                    transpose_x(u, h)

            pe.wait_ge(const_ready, 2)
            with pe.Fori(0, WARM_UP):
                pe.matmul(bank[:, 7, 0:P], ident[:], ident[:], start=True, stop=True)
            pe.wait_ge(got_cond, 16)
            pe.transpose(condT_b_ps[:, 0:B], cond_sb[:], ident[:])
            pe.wait_ge(got_b, 16 * 2)
            pe.transpose(condT_b_ps[:, B:B + 2 * DC], b_rows[:], ident[0:2 * DC, 0:2 * DC]).then_inc(condT_done, 1)
            pe.wait_ge(got_x0, 16)
            transpose_x(0, 0)
            pe.wait_ge(got_W3, 16)
            pe.wait_ge(condT_copied, 1)
            for c in range(DC):
                pe.matmul(qT_ps[:, c, :], W3_sb[:, c * P:(c + 1) * P], condT, start=True, stop=True
                          ).then_inc(q_done, 1)
            pe.wait_ge(got_xs[0], 16)
            transpose_x(0, 1)
            pe.wait_ge(got_xs[1], 16)
            for h in range(HALVES):
                transpose_x(1, h)
            pe.wait_ge(got_W2, 16)
            pe.wait_ge(q_ready, DC)
            with pe.Fori(0, NG // 4) as i:
                for u in range(2):
                    project_c(i * 2 + u, u)
                    transpose_next(i * 2 + u, u, i + 1)

            def sum_partitions(b, cols, rest):
                pe.matmul(sums_ps[b], ones[:], abs_sums[:, cols], start=True, stop=False, skip_group_check=True)
                pe.matmul(sums_ps[b][:, 0:1], ones[:], abs_sums[:, rest], start=False, stop=True,
                          skip_group_check=True).then_inc(sums_done, 1)

            pe.wait_ge(const_ready, 4)
            pe.wait_ge(w1_abs_done, 2)
            sum_partitions(0, slice(0, 1), slice(3, 4))
            for g in range(NG // 2, NG - 2):
                project_c(g, g % 2)
                transpose_next(g, g % 2, g // 2 + 1)
            pe.wait_ge(abs_done, 3)
            sum_partitions(1, slice(1, 3), slice(4, 5))

            def transpose_w(k, w_t):
                pe.wait_ge(ternary_done, k + 1)
                for c in range(DC):
                    pe.wait_ge(scale_step, 1 + c) if k == 0 else pe.wait_ge(wT_copied, c + 1)
                    for j in range(STEPS):
                        rows = P if j < HC else HR
                        last = pe.transpose(w_ps[c][:, j * P:j * P + rows], w_t[0:rows, j, c * P:(c + 1) * P],
                                            ident16[0:rows, 0:rows])
                last.then_inc(wT_done, 1)

            project_c(NG - 2, 0)
            transpose_w(0, w1_t)
            project_c(NG - 1, 1)
            transpose_w(1, w3_t)

            def hidden_product(g, j, dst, col, done):
                w = P if j < HC else RM
                passes = [(k, part) for k in range(DC) for part in (c_hi, c_lo)]
                for i, (k, part) in enumerate(passes):
                    last = pe.matmul(dst[j % 3][0:w, :], T13[:, k, col:col + w], part[:, at(g), k, :],
                                     start=(i == 0), stop=(i == len(passes) - 1))
                last.then_inc(done, 1)

            def h1_step(g, j):
                hidden_product(g, j, h1, j * P, h1_done)

            def h3_step(g, j):
                hidden_product(g, j, h3, (HC + j) * P, h3_done)

            def hidden_step(g, j):
                if j < HC:
                    h1_step(g, j)
                    h3_step(g, j)
                else:
                    hidden_product(g, j, h1, 2 * HC * P, h1_done)

            def output_share(g, j, b, tiles):
                pe.wait_ge(g_lo_done, g * STEPS + j + 1)
                parts = [(g_hi[j], P), (g_lo[j], P)] if j < HC else [(g_rest, RM)]
                if j == 0:
                    pe.wait_ge(T2_copied, 4)
                    pe.wait_ge(o_free[b], g + 1)
                for i, (part, rows) in enumerate(parts):
                    for n, (t, out_ps) in enumerate(tiles.items()):
                        last = pe.matmul(out_ps, part[0:rows, t * P:(t + 1) * P], T2[0:rows, j, :],
                                         start=(j == 0 and i == 0 and n == 0), stop=(j == HC),
                                         skip_group_check=True)
                if j == HC:
                    last.then_inc(o_done[b], 1)

            def output_step(g, j):
                for b in range(TT // 2):
                    output_share(g, j, b, {2 * b + t: o[b][:, t, :] for t in range(2)})

            pe.wait_ge(wT_copied, DC)
            pe.wait_ge(ct_free, 2 + NG // 2)
            pe.wait_ge(y_done, NG * HALVES)
            for j in range(2):
                h1_step(0, j)
            pe.wait_ge(wT_copied, 2 * DC)
            h3_step(0, 0)
            pe.wait_ge(ternary_done, 3)
            for j in range(STEPS):
                rows = P if j < HC else HR
                for c in range(DC):
                    col = (j % W2_HALF) * D + c * P
                    last = pe.transpose(w_ps[j // W2_HALF][0:rows, col:col + P], w2_t[:, c, j * P:j * P + rows],
                                        ident16[:])
            last.then_inc(wT_done, 1)
            h3_step(0, 1)
            for c in range(DC):
                pe.wait_ge(z_free[c], NG + 1)
            hidden_step(0, 2)
            with pe.Fori(0, NG - 1) as g:
                for j in range(STEPS):
                    pe.wait_ge(g_done, g * STEPS + j + 1)
                    if j + 3 == STEPS:
                        pe.wait_ge(late_lo_done, NG // 2)
                    hidden_step(*later(g, j, 3))
                    for done in output_after(j):
                        output_step(g, done)
            for j in range(STEPS - 3):
                pe.wait_ge(g_done, (NG - 1) * STEPS + j + 1)
                hidden_step(NG - 1, j + 3)
            last_tiles = [(0, {0: o[0][:, 0, :], 1: o[0][:, 1, :]}), (1, {2: o[1][:, 0, :]}), (1, {3: o_last})]
            for j in range(STEPS - 3):
                for b, tiles in last_tiles:
                    output_share(NG - 1, j, b, tiles)
            for b, tiles in last_tiles:
                for j in range(STEPS - 3, STEPS):
                    output_share(NG - 1, j, b, tiles)

        @block.vector
        def _(dve):
            def sum_and_add(g, u, before=True, halves=range(HALVES)):
                for h in halves:
                    dve.wait_ge(xT_done, g * HALVES + h + 1)
                    nc.vector.tensor_reduce(vsum[u][:, h, :], by_batch(xT[u][h]), AX.X, ALU.add).then_inc(vsum_done, 1)
                    dve.wait_ge(vsum_done, g * HALVES + h + 1)
                    if before:
                        dve.wait_ge(x1_done, (g - 2) * HALVES + h + 1)
                    nc.vector.scalar_tensor_tensor(
                        out=by_batch(flat(y[u][:, h])), in0=by_batch(xT[u][h]), scalar=float(S),
                        in1=over_sequence(vsum[u][:, h, :]), op0=ALU.mult, op1=ALU.add).then_inc(y_done, 1)

            def lo_of_c(g, u):
                dve.wait_ge(c_hi_done, g + 1)
                nc.vector.tensor_tensor(group_of(c_lo, g), ct[u][:], group_of(c_hi, g).bitcast(F32), ALU.subtract
                                        ).then_inc(ct_free, 1)

            def pieces(k):
                return [(slice(0, P), slice(0, HC * D)), (slice(0, HR), slice(HC * D, STEPS * D))] if k < 2 else \
                    [(slice(0, P), slice(0, DC * H))]

            def flat_weight(w):
                return w[:].rearrange("p a b -> p (a b)")

            def below_limit(w_sb, k):
                for rows, cols in pieces(k):
                    nc.vector.tensor_scalar(below[rows, cols], flat_weight(w_sb)[rows, cols],
                                            neg_limits[rows, k:k + 1], None, ALU.is_lt).then_inc(below_done, 1)

            def ternary(w_sb, w_t, k):
                dve.wait_ge(below_done, sum(len(pieces(i)) for i in range(k + 1)))
                for rows, cols in pieces(k):
                    last = nc.vector.scalar_tensor_tensor(
                        out=flat_weight(w_t)[rows, cols], in0=flat_weight(w_sb)[rows, cols],
                        scalar=limits[rows, k:k + 1], in1=below[rows, cols], op0=ALU.is_gt, op1=ALU.subtract)
                last.then_inc(ternary_done, 1)

            sum_and_add(0, 0, before=False)
            sum_and_add(1, 1, before=False)
            dve.wait_ge(got_w1, 32)
            dve.wait_ge(zeroed, 1)
            for rows, chunks, col in ((P, slice(0, HC), 0), (HR, slice(HC, STEPS), 3)):
                nc.vector.tensor_reduce(abs_sums[0:rows, col:col + 1], w1_sb[0:rows, chunks, :], AX.XY, ALU.add,
                                        apply_absolute_value=True).then_inc(w1_abs_done, 1)
            with dve.Fori(0, NG // 4) as i:
                for u in range(2):
                    sum_and_add(i * 2 + u + 2, u)
                    lo_of_c(i * 2 + u, u)

            def scale_and_limits(b, own):
                dve.wait_ge(sums_done, b + 1)
                for dst, factor in ((scales, 1.0), (limits, 0.5), (neg_limits, -0.5)):
                    last = nc.vector.tensor_scalar(dst[:, own], sums_ps[b], factor / W_COUNT, None, ALU.mult)
                last.then_inc(scale_step, 1)

            scale_and_limits(0, slice(0, 1))
            sum_and_add(NG - 2, 0)
            dve.wait_ge(abs_done, 2)
            dve.wait_ge(scale_step, 1)
            below_limit(w1_sb, 0)
            sum_and_add(NG - 1, 1, halves=[0])
            ternary(w1_sb, w1_t, 0)
            scale_and_limits(1, slice(1, 3))
            sum_and_add(NG - 1, 1, halves=[1])
            dve.wait_ge(scale_step, 2)
            for k, w_sb, w_t in ((1, w3_sb, w3_t), (2, w2_sb, w2_t)):
                dve.wait_ge(ternary_done, k)
                below_limit(w_sb, k)
                ternary(w_sb, w_t, k)
            nc.vector.reciprocal(inverse[:], scales[:]).then_inc(scale_step, 1)
            dve.wait_ge(scale_step, 3)
            nc.vector.scalar_tensor_tensor(out=checked[:], in0=inverse[:], scalar=0.0, in1=scales[:],
                                           op0=ALU.mult, op1=ALU.add).then_inc(scale_step, 1)
            dve.wait_ge(scale_step, 4)
            nc.vector.tensor_tensor(out_scale[:], checked[:, 1:2], checked[:, 2:3], ALU.mult).then_inc(scale_step, 1)
            dve.wait_ge(scale_step, 5)

            def g_step(g, j):
                n, r = g * STEPS + j, rows_of(j)
                dve.wait_ge(silu_done, n + 1)
                if not (isinstance(g, int) and g == 0 and j < 3):
                    dve.wait_ge(g_lo_done, n - 2)
                if j < HC:
                    dve.wait_ge(h3_done, g * HC + j + 1)
                second = h3[j % 3] if j < HC else h1[j % 3][HR2:RM, :]
                nc.vector.tensor_tensor(gf[j % 3][r], silu[j % 2][r], second, ALU.mult).then_inc(g_done, 1)

            def lo_step(g, j):
                dve.wait_ge(g_hi_done, g * STEPS + j + 1)
                hi = g_hi[j][:] if j < HC else g_rest[0:HR, :]
                lo = g_lo[j][:] if j < HC else g_rest[HR2:RM, :]
                nc.vector.tensor_tensor(lo, gf[j % 3][rows_of(j)], hi.bitcast(F32), ALU.subtract).then_inc(g_lo_done, 1)

            def residual(g, b, out_ps, t0, t1, done):
                dve.wait_ge(o_done[b], done)
                xg = xo[:, at(g), t0:t1, :]
                xg = xg if isinstance(g, int) else xg.rearrange("p a t d -> p (a t) d")
                nc.vector.scalar_tensor_tensor(out=xg, in0=out_ps, scalar=out_scale[:, 0:1], in1=xg,
                                               op0=ALU.mult, op1=ALU.add).then_inc(o_free[b], 1)

            g_step(0, 0)
            dve.wait_ge(wT_done, 3)
            nc.vector.tensor_copy(T2[:, 0:W2_HALF, :], w_ps[0][:, 0:W2_HALF * D].rearrange("p (j d) -> p j d", d=D)
                                  ).then_inc(T2_copied, 1)
            g_step(0, 1)
            lo_step(0, 0)
            g_step(0, 2)
            lo_step(0, 1)
            dve.wait_ge(got_xo, 16)
            with dve.Fori(0, NG - 1) as g:
                for j in range(STEPS):
                    g_step(*later(g, j, 3))
                    lo_step(*later(g, j, 2))
                for b in range(TT // 2):
                    residual(g, b, o[b], 2 * b, 2 * b + 2, g + 1)
            for j in range(STEPS):
                if j + 3 < STEPS:
                    g_step(NG - 1, j + 3)
                if j + 2 < STEPS:
                    lo_step(NG - 1, j + 2)
            residual(NG - 1, 0, o[0], 0, 2, NG)
            residual(NG - 1, 1, o[1][:, 0:1, :], 2, 3, NG)
            residual(NG - 1, 1, o_last.unsqueeze(1), 3, 4, NG + 1)


_INS = ["x", "cond_1024", "L0_cond_W3", "L0_cond_b3", "L0_cond_W2", "L0_cond_b2", "L0_ffn_w1", "L0_ffn_w3", "L0_ffn_w2"]
_OUTS = [((128, 32, 256), "float32")]


def kernel(**inputs):
    import numpy as _np
    import concourse.bacc as _bacc
    from concourse import mybir as _mybir
    from concourse.bass_utils import run_bass_kernel_spmd as _run

    nc = _bacc.Bacc("TRN2", target_bir_lowering=False, num_devices=1)
    arrays, args = {}, []
    for name in _INS:
        a = _np.ascontiguousarray(inputs[name])
        arrays[f"in_{name}_dram"] = a
        args.append(nc.dram_tensor(f"in_{name}_dram", a.shape, _mybir.dt.from_np(a.dtype), kind="ExternalInput").ap())
    for i, (shape, dtype) in enumerate(_OUTS):
        dt = _mybir.dt.from_np(_np.dtype(dtype))
        args.append(nc.dram_tensor(f"out_{i}_dram", shape, dt, kind="ExternalOutput").ap())
    adaln_ternary_ffn_kernel(nc, *args)
    r = _run(nc, [arrays], core_ids=[0])
    return r.results[0]["out_0_dram"]
```
